# Optimizing a Trainium2 kernel written in Bass

```python
import numpy as np
import jax
import jax.numpy as jnp

def _softmax(x, axis=-1):
    return jax.nn.softmax(x, axis=axis)

def _gelu(x):
    return jax.nn.gelu(x, approximate=True)

def _silu(x):
    return jax.nn.silu(x)

def _sigmoid(x):
    return jax.nn.sigmoid(x)

def _layernorm(x, axis=-1, eps=1e-05):
    m = jnp.mean(x, axis=axis, keepdims=True)
    v = jnp.var(x, axis=axis, keepdims=True)
    return (x - m) / jnp.sqrt(v + eps)

def _scatter_add(tgt, idx, src, axis=0):
    return tgt.at[idx].add(src)

def _segment_sum(src, seg, n):
    return jax.ops.segment_sum(src, seg, n)
kernel_name = 'mk_adj_resnorm_d2_adj_r2_2b12ed'

def setup_inputs(seed: int=0):
    np.random.seed(seed)
    _w = jnp.asarray

    def _rec_inputs():
        import jax
        import jax.numpy as jnp
        _gk = jax.random.key(seed)
        x = -0.000929 + 1 * jax.random.normal(jax.random.fold_in(_gk, 1), (2048, 128), jnp.float32)
        _w = (1.0 + jnp.arange(2048, dtype=jnp.float32)) ** (-0.5)
        _w = _w / _w.mean()
        _pij = jnp.clip(0.000976562 * _w[:, None] * _w[None, :], 0.0, 1.0)
        _a = jax.random.uniform(jax.random.fold_in(_gk, 2), (2048, 2048)) < _pij
        _a = jnp.logical_or(_a, jnp.eye(2048, dtype=bool))
        _af = _a.astype(jnp.float32)
        _af = _af * jax.random.uniform(jax.random.fold_in(_gk, 3), (2048, 2048), jnp.float32, 0.05, 1)
        adj = _af
        return (x, adj)
    x, adj = _rec_inputs()

    def _L0_gnn_setup():
        import jax, jax.numpy as jnp
        import numpy as np
        N = 4096
        D = 128
        key = jax.random.key(seed)
        kx, ka, kw1, kw2 = jax.random.split(key, 4)
        x = jax.random.normal(kx, (N, D), dtype=jnp.float32)
        A = jax.random.uniform(ka, (N, N), dtype=jnp.float32)
        s = 0.05
        W1 = jax.random.normal(kw1, (D, D), dtype=jnp.float32) * s
        b1 = jnp.zeros((D,), dtype=jnp.float32)
        W2 = jax.random.normal(kw2, (D, D), dtype=jnp.float32) * s
        b2 = jnp.zeros((D,), dtype=jnp.float32)
        return {'x': x, 'A': A, 'W1': W1, 'b1': b1, 'W2': W2, 'b2': b2}
    _L0_gnn_all = _L0_gnn_setup()
    _L0_gnn_in = {k: v for k, v in _L0_gnn_all.items() if k in ('W1', 'b1', 'W2', 'b2')}
    del _L0_gnn_all

    def _L1_gnn_setup():
        import jax, jax.numpy as jnp
        import numpy as np
        N = 4096
        F_IN = 128
        FILTERS = 128
        EDGE_PROB = 0.004
        key = jax.random.key(seed)
        k_x, k_a, k_w1, k_w2, k_w3 = jax.random.split(key, 5)
        x = jax.random.normal(k_x, (N, F_IN), dtype=jnp.float32)
        A = (jax.random.uniform(k_a, (N, N)) < EDGE_PROB).astype(jnp.float32)
        scale = 1.0 / np.sqrt(F_IN)
        W1 = jax.random.normal(k_w1, (F_IN, FILTERS), dtype=jnp.float32) * scale
        W2 = jax.random.normal(k_w2, (F_IN, FILTERS), dtype=jnp.float32) * scale
        W3 = jax.random.normal(k_w3, (F_IN, FILTERS), dtype=jnp.float32) * scale
        return {'x': x, 'A': A, 'W1': W1, 'W2': W2, 'W3': W3}
    _L1_gnn_all = _L1_gnn_setup()
    _L1_gnn_in = {k: v for k, v in _L1_gnn_all.items() if k in ('W1', 'W2', 'W3')}
    del _L1_gnn_all
    return {'x': x, 'adj': adj, 'L0_gnn_W1': _L0_gnn_in['W1'], 'L0_gnn_b1': _L0_gnn_in['b1'], 'L0_gnn_W2': _L0_gnn_in['W2'], 'L0_gnn_b2': _L0_gnn_in['b2'], 'L1_gnn_W1': _L1_gnn_in['W1'], 'L1_gnn_W2': _L1_gnn_in['W2'], 'L1_gnn_W3': _L1_gnn_in['W3']}

def reference(x, adj, L0_gnn_W1, L0_gnn_b1, L0_gnn_W2, L0_gnn_b2, L1_gnn_W1, L1_gnn_W2, L1_gnn_W3):
    import jax
    import jax.numpy as jnp

    def _L0_gnn_ref(x, A, W1, b1, W2, b2):
        import jax, jax.numpy as jnp
        import numpy as np
        N = 4096
        D = 128
        h = jax.nn.relu(jnp.matmul(A, jnp.matmul(x, W1)) + b1)
        h = jax.nn.relu(jnp.matmul(A, jnp.matmul(h, W2)) + b2)
        return h

    def _L1_gnn_ref(x, A, W1, W2, W3):
        import jax, jax.numpy as jnp
        import numpy as np
        N = 4096
        F_IN = 128
        FILTERS = 128
        EDGE_PROB = 0.004
        A2 = A @ A
        A3 = A2 @ A
        f1 = A @ x @ W1
        f2 = A2 @ x @ W2
        f3 = A3 @ x @ W3
        return (f1 + f2 + f3) / 3.0
    x = _layernorm(x + _L0_gnn_ref(x, adj, L0_gnn_W1, L0_gnn_b1, L0_gnn_W2, L0_gnn_b2), axis=-1)
    x = _layernorm(x + _L1_gnn_ref(x, adj, L1_gnn_W1, L1_gnn_W2, L1_gnn_W3), axis=-1)
    return x

_drawn_inputs = setup_inputs


def setup_inputs(seed=0):
    import zlib

    import numpy as np

    out = dict(_drawn_inputs(seed))
    spreads = {'L0_gnn_b1': (0.0, 0.1), 'L0_gnn_b2': (0.0, 0.1)}
    factors = {}
    for name, (base, spread) in spreads.items():
        noise = np.random.default_rng([zlib.crc32(name.encode()), seed]).standard_normal(out[name].shape)
        drawn = base * np.exp(spread * noise) if base else spread * noise
        out[name] = jnp.asarray(drawn.astype(out[name].dtype))
    for name, factor in factors.items():
        out[name] = (out[name] * factor).astype(out[name].dtype)
    return out
```

```python
from contextlib import ExitStack

import concourse.bass as bass
from concourse import mybir

P = 128
N = 2048
D = 128
TILES = N // P
CHUNK = 512
CHUNKS = N // CHUNK
TPC = CHUNK // P
HOPS = 5
NORMED = (1, 4)
POST_AT = 2
EPS = 1e-5

F32 = mybir.dt.float32
ALU = mybir.AluOpType
ACT = mybir.ActivationFunctionType

W1, W2, V1, V2, V3, B1, B2 = 0, D, 2 * D, 3 * D, 4 * D, 5 * D, 5 * D + 1
PARAMS = 5 * D + 2
NORM_STEPS = 5


def graph_layers(nc: bass.Bass, a_t, x_t, x_rows, params, out_rows):
    with ExitStack() as ctx:
        def sb(name, shape, dt=F32):
            return ctx.enter_context(nc.sbuf_tensor(name, shape, dt))

        def psum(name, shape, dt=F32):
            return ctx.enter_context(nc.psum_tensor(name, shape, dt))

        def sem(name):
            return ctx.enter_context(nc.semaphore(name))

        adj = sb("adj", [P, CHUNKS, TILES, CHUNK])
        nodes = sb("nodes", [P, TILES, D])
        operand = sb("operand", [P, 2, TILES, D])
        xt = sb("xt", [P, N])
        par = sb("par", [P, PARAMS])
        ident = sb("ident", [P, P])
        chunk_t = sb("chunk_t", [P, CHUNK])
        stats = sb("stats", [P, TPC, 6])
        moments = sb("moments", [P, TPC, 2])
        deviation = sb("deviation", [P, TPC])
        rstd = sb("rstd", [P, TPC])

        sums = psum("sums", [P, CHUNKS, CHUNK])
        turned = psum("turned", [P, TPC, D])
        weighted = psum("weighted", [P, TPC, D])

        adj_in = [sem(f"adj_in{j}") for j in range(CHUNKS)]
        x_t_in = sem("x_t_in")
        x_in = sem("x_in")
        params_in = sem("params_in")
        ident_zero = sem("ident_zero")
        ident_ready = sem("ident_ready")
        chunk_summed = sem("chunk_summed")
        chunk_evacuated = sem("chunk_evacuated")
        post_multiplied = sem("post_multiplied")
        taken_over = sem("taken_over")
        first_multiplied = sem("first_multiplied")
        residual_added = sem("residual_added")
        norm_step = sem("norm_step")
        deviation_ready = sem("deviation_ready")
        out_stored = sem("out_stored")

        block = ctx.enter_context(nc.Block())

        def groups_of(hop, c):
            return operand[:, hop % 2, bass.ts(c, TPC), :]

        @block.sync
        def _(sp):
            sp.dma_start(par[:], params).then_inc(params_in, 16)
            sp.dma_start(xt[:], x_t).then_inc(x_t_in, 16)
            for c in range(CHUNKS):
                for j in range(TILES // TPC):
                    if c >= 1:
                        sp.wait_ge(adj_in[j], 16 * c)
                    sp.dma_start(adj[:, c, j * TPC:(j + 1) * TPC, :],
                                 a_t[c, :, j * TPC:(j + 1) * TPC, :]).then_inc(adj_in[j], 16)
                if c == 0:
                    sp.dma_start(nodes[:], x_rows).then_inc(x_in, 16)
            for c in range(CHUNKS):
                sp.wait_ge(norm_step, (CHUNKS + c + 1) * NORM_STEPS)
                sp.dma_start(out_rows[:, c * TPC:(c + 1) * TPC, :],
                             nodes[:, c * TPC:(c + 1) * TPC, :]).then_inc(out_stored, 16)
            sp.wait_ge(out_stored, 16 * CHUNKS)

        @block.gpsimd
        def _(pool):
            nc.gpsimd.memset(ident[:], 0.0).then_inc(ident_zero, 1)
            pool.wait_ge(ident_zero, 1)
            nc.gpsimd.affine_select(out=ident[:], in_=ident[:], compare_op=ALU.not_equal, fill=1.0, base=0,
                                    pattern=[[-1, P]], channel_multiplier=1).then_inc(ident_ready, 1)

        @block.tensor
        def _(pe):
            def post(hop, c):
                g = hop * CHUNKS + c
                pe.wait_ge(chunk_evacuated, g + 1)
                pe.wait_ge(taken_over, CHUNKS + g)
                for t in range(TPC):
                    tile = chunk_t[:, t * P:(t + 1) * P]
                    if hop in (1, 2, 3):
                        last = nc.tensor.transpose(turned[:, t, :], tile, ident[:])
                    if hop != 1:
                        w = {0: W2, 2: V1, 3: V2, 4: V3}[hop]
                        last = nc.tensor.matmul(weighted[:, t, :], tile, par[:, w:w + D], start=True, stop=True)
                last.then_inc(post_multiplied, 1)

            def chunk(hop, c, before):
                for k in range(TILES):
                    if hop == 0 and k % TPC == 0:
                        pe.wait_ge(adj_in[k // TPC], 16 * c + 16)
                    if isinstance(c, int) and c == 0 and k % TPC == 0:
                        pe.wait_ge(taken_over, hop * CHUNKS + k // TPC + 1)
                    if k == POST_AT and before:
                        post(*before)
                    last = nc.tensor.matmul(sums[:, c, :], operand[:, hop % 2, k, :], adj[:, c, k, :],
                                            start=(k == 0), stop=(k == TILES - 1))
                last.then_inc(chunk_summed, 1)

            pe.wait_ge(params_in, 16)
            pe.wait_ge(x_t_in, 16)
            for g in range(CHUNKS):
                for t in range(TPC):
                    last = nc.tensor.matmul(sums[:, g, t * D:(t + 1) * D], xt[:, (g * TPC + t) * P:(g * TPC + t + 1) * P],
                                            par[:, W1:W1 + D], start=True, stop=True)
                last.then_inc(first_multiplied, 1)
            pe.wait_ge(ident_ready, 1)
            for hop in range(HOPS):
                chunk(hop, 0, (hop - 1, CHUNKS - 1) if hop else None)
                with pe.Fori(1, CHUNKS) as c:
                    chunk(hop, c, (hop, c - 1))
            post(HOPS - 1, CHUNKS - 1)

        @block.scalar
        def _(act):
            def deviations(n):
                act.wait_ge(norm_step, n * NORM_STEPS + 3)
                nc.scalar.activation(deviation[:], moments[:, :, 1], ACT.Sqrt).then_inc(deviation_ready, 1)

            def chunk(hop, c):
                g = hop * CHUNKS + c
                act.wait_ge(chunk_summed, g + 1)
                if hop == 0:
                    nc.scalar.activation(chunk_t[:], sums[:, c, :], ACT.Relu, bias=par[:, B1:B1 + 1]
                                         ).then_inc(chunk_evacuated, 1)
                elif hop == 1:
                    nc.scalar.activation(chunk_t[:], sums[:, c, :], ACT.Relu, bias=par[:, B2:B2 + 1]
                                         ).then_inc(chunk_evacuated, 1)
                    deviations(c)
                else:
                    nc.scalar.activation(chunk_t[:], sums[:, c, :], ACT.Copy).then_inc(chunk_evacuated, 1)
                if hop == HOPS - 1:
                    deviations(CHUNKS + c)

            for hop in range(HOPS):
                with act.Fori(0, CHUNKS) as c:
                    chunk(hop, c)

        @block.vector
        def _(dve):
            def normalise(n, c):
                step = n * NORM_STEPS
                for t in range(TPC):
                    last = nc.vector.bn_stats(stats[:, t, :], nodes[:, bass.ds(c * TPC + t, 1), :])
                last.then_inc(norm_step, 1)
                dve.wait_ge(norm_step, step + 1)
                for t in range(TPC):
                    last = nc.vector.bn_aggr(moments[:, t, :], stats[:, t, :])
                last.then_inc(norm_step, 1)
                dve.wait_ge(norm_step, step + 2)
                nc.vector.tensor_scalar(moments[:, :, 1], moments[:, :, 1], EPS, None, ALU.add).then_inc(norm_step, 1)
                dve.wait_ge(deviation_ready, n + 1)
                nc.vector.reciprocal(rstd[:], deviation[:]).then_inc(norm_step, 1)
                dve.wait_ge(norm_step, step + 4)
                for t in range(TPC):
                    tile = nodes[:, bass.ds(c * TPC + t, 1), :]
                    last = nc.vector.tensor_scalar(tile, tile, moments[:, t, 0:1], rstd[:, t:t + 1],
                                                   ALU.subtract, ALU.mult)
                last.then_inc(norm_step, 1)

            def chunk(hop, c):
                g = hop * CHUNKS + c
                group = nodes[:, bass.ts(c, TPC), :]
                laid = operand[:, (hop + 1) % 2, bass.ts(c, TPC), :]
                dve.wait_ge(post_multiplied, g + 1)
                if hop == 0:
                    nc.vector.tensor_copy(laid, weighted[:]).then_inc(taken_over, 1)
                elif hop == 1:
                    nc.vector.tensor_tensor(group, turned[:], group, ALU.add).then_inc(residual_added, 1)
                    dve.wait_ge(residual_added, c + 1)
                    normalise(c, c)
                    dve.wait_ge(norm_step, (c + 1) * NORM_STEPS)
                    nc.vector.tensor_copy(laid, group).then_inc(taken_over, 1)
                elif hop < HOPS - 1:
                    nc.vector.tensor_copy(laid, turned[:])
                    nc.vector.scalar_tensor_tensor(group, weighted[:], 1.0 / 3.0, group, ALU.mult, ALU.add
                                                   ).then_inc(taken_over, 1)
                else:
                    nc.vector.scalar_tensor_tensor(group, weighted[:], 1.0 / 3.0, group, ALU.mult, ALU.add
                                                   ).then_inc(taken_over, 1)
                    dve.wait_ge(taken_over, CHUNKS + g + 1)
                    normalise(c + CHUNKS, c)

            for g in range(CHUNKS):
                dve.wait_ge(first_multiplied, g + 1)
                nc.vector.tensor_copy(operand[:, 0, g * TPC:(g + 1) * TPC, :], sums[:, g, :]).then_inc(taken_over, 1)
            dve.wait_ge(x_in, 16)
            for hop in range(HOPS):
                if hop in NORMED:
                    for c in range(CHUNKS):
                        chunk(hop, c)
                else:
                    with dve.Fori(0, CHUNKS) as c:
                        chunk(hop, c)


def kernel(x, adj, L0_gnn_W1, L0_gnn_b1, L0_gnn_W2, L0_gnn_b2, L1_gnn_W1, L1_gnn_W2, L1_gnn_W3):
    import numpy as np
    import concourse.bacc as bacc
    from concourse.bass_utils import run_bass_kernel_spmd

    x, adj = np.asarray(x), np.asarray(adj)
    arrays = {
        "a_t": adj.reshape(CHUNKS, CHUNK, TILES, P).transpose(0, 3, 2, 1),
        "x_t": x.T,
        "x_rows": x.reshape(TILES, P, D).transpose(1, 0, 2),
        "params": np.concatenate([np.asarray(L0_gnn_W1), np.asarray(L0_gnn_W2), np.asarray(L1_gnn_W1),
                                  np.asarray(L1_gnn_W2), np.asarray(L1_gnn_W3),
                                  np.asarray(L0_gnn_b1)[:, None], np.asarray(L0_gnn_b2)[:, None]], axis=1),
    }
    arrays = {name: np.ascontiguousarray(a) for name, a in arrays.items()}
    nc = bacc.Bacc("TRN2", target_bir_lowering=False, num_devices=1)
    ins = [nc.dram_tensor(name, a.shape, F32, kind="ExternalInput").ap() for name, a in arrays.items()]
    out_rows = nc.dram_tensor("out_rows", (P, TILES, D), F32, kind="ExternalOutput").ap()
    graph_layers(nc, *ins, out_rows)
    r = run_bass_kernel_spmd(nc, [arrays], core_ids=[0])
    return np.asarray(r.results[0]["out_rows"]).transpose(1, 0, 2).reshape(N, D)
```

```python
from contextlib import ExitStack

import concourse.bass as bass
from concourse import mybir

P = 128
N = 2048
D = 128
TILES = N // P
CHUNK = 512
CHUNKS = N // CHUNK
TPC = CHUNK // P
GROUPS = 4
STREAMED = TILES // GROUPS - 1
BLOCKS = GROUPS * STREAMED
RING = 4
HOPS = 5
NORMED = (1, 4)
WEIGHTED = (0, 2, 3, 4)
TURNED = (1, 2, 3)
POST_AT = 2
EVACUATE_AT = RING
NORM_STEPS = 5
EPS = 1e-5
assert BLOCKS % RING == 0 and TPC == GROUPS == CHUNKS

F32 = mybir.dt.float32
F32R = mybir.dt.float32r
ALU = mybir.AluOpType
ACT = mybir.ActivationFunctionType

W1, W2, V1, V2, V3, B1, B2 = 0, D, 2 * D, 3 * D, 4 * D, 5 * D, 5 * D + 1
PARAMS = 5 * D + 2


def graph_layers(nc: bass.Bass, a_t, x_t, x_rows, params, out_rows):
    with ExitStack() as ctx:
        def sb(name, shape, dt=F32):
            return ctx.enter_context(nc.sbuf_tensor(name, shape, dt))

        def psum(name, shape, dt=F32):
            return ctx.enter_context(nc.psum_tensor(name, shape, dt))

        def sem(name):
            return ctx.enter_context(nc.semaphore(name))

        adj = sb("adj", [P, CHUNKS, BLOCKS, CHUNK])
        resident_high = sb("resident_high", [P, CHUNKS, GROUPS, CHUNK], F32R)
        resident_low = sb("resident_low", [P, CHUNKS, GROUPS, CHUNK], F32R)
        ring_high = sb("ring_high", [P, RING, CHUNK], F32R)
        ring_low = sb("ring_low", [P, RING, CHUNK], F32R)
        operand_high = sb("operand_high", [P, 2, TILES, D], F32R)
        operand_low = sb("operand_low", [P, 2, TILES, D], F32R)
        nodes = sb("nodes", [P, TILES, D])
        par = sb("par", [P, PARAMS])
        ident = sb("ident", [P, P])
        chunk_t = sb("chunk_t", [P, CHUNK])
        stats = sb("stats", [P, TPC, 6])
        moments = sb("moments", [P, TPC, 2])
        deviation = sb("deviation", [P, TPC])
        rstd = sb("rstd", [P, TPC])
        xt = nodes[:].rearrange("p t d -> p (t d)")
        staged = nodes[:].rearrange("p (j t) d -> p j (t d)", j=GROUPS)

        sums = psum("sums", [P, CHUNKS, CHUNK])
        turned = psum("turned", [P, TPC, D])
        weighted = psum("weighted", [P, TPC, D])

        adj_in = [sem(f"adj_in{j}") for j in range(GROUPS)]
        x_t_in = sem("x_t_in")
        x_in = sem("x_in")
        params_in = sem("params_in")
        ident_zero = sem("ident_zero")
        ident_ready = sem("ident_ready")
        high_ready = sem("high_ready")
        low_ready = sem("low_ready")
        block_used = sem("block_used")
        resident_high_ready = sem("resident_high_ready")
        resident_low_ready = sem("resident_low_ready")
        first_multiplied = sem("first_multiplied")
        chunk_summed = sem("chunk_summed")
        chunk_evacuated = sem("chunk_evacuated")
        post_multiplied = sem("post_multiplied")
        operand_high_ready = sem("operand_high_ready")
        taken_over = sem("taken_over")
        residual_added = sem("residual_added")
        norm_step = sem("norm_step")
        deviation_ready = sem("deviation_ready")
        out_stored = sem("out_stored")

        block = ctx.enter_context(nc.Block())

        @block.sync
        def _(sp):
            sp.dma_start(xt, x_t).then_inc(x_t_in, 16)
            sp.dma_start(par[:], params).then_inc(params_in, 16)
            for c in range(CHUNKS):
                for j in range(GROUPS):
                    k = j * (STREAMED + 1)
                    if c >= 1:
                        sp.wait_ge(adj_in[j], 32 * c)
                    sp.dma_start(adj[:, c, j * STREAMED:(j + 1) * STREAMED, :],
                                 a_t[c, :, k:k + STREAMED, :]).then_inc(adj_in[j], 16)
                    if c == 0 and j == 0:
                        sp.wait_ge(first_multiplied, CHUNKS)
                    if c >= 1:
                        sp.wait_ge(resident_low_ready, (c - 1) * GROUPS + j + 1)
                    sp.dma_start(staged[:, j, :], a_t[c, :, k + STREAMED, :]).then_inc(adj_in[j], 16)
            sp.wait_ge(resident_low_ready, CHUNKS * GROUPS)
            sp.dma_start(nodes[:], x_rows).then_inc(x_in, 16)
            for c in range(CHUNKS):
                sp.wait_ge(norm_step, (CHUNKS + c + 1) * NORM_STEPS)
                sp.dma_start(out_rows[:, c * TPC:(c + 1) * TPC, :],
                             nodes[:, c * TPC:(c + 1) * TPC, :]).then_inc(out_stored, 16)
            sp.wait_ge(out_stored, 16 * CHUNKS)

        @block.gpsimd
        def _(pool):
            nc.gpsimd.memset(ident[:], 0.0).then_inc(ident_zero, 1)
            pool.wait_ge(ident_zero, 1)
            nc.gpsimd.affine_select(out=ident[:], in_=ident[:], compare_op=ALU.not_equal, fill=1.0, base=0,
                                    pattern=[[-1, P]], channel_multiplier=1).then_inc(ident_ready, 1)

        @block.tensor
        def _(pe):
            def post(hop, c):
                g = hop * CHUNKS + c
                pe.wait_ge(chunk_evacuated, g + 1)
                pe.wait_ge(taken_over, CHUNKS + g)
                for t in range(TPC):
                    tile = chunk_t[:, t * P:(t + 1) * P]
                    if hop in TURNED:
                        last = nc.tensor.transpose(turned[:, t, :], tile, ident[:])
                    if hop in WEIGHTED:
                        w = {0: W2, 2: V1, 3: V2, 4: V3}[hop]
                        last = nc.tensor.matmul(weighted[:, t, :], tile, par[:, w:w + D], start=True, stop=True)
                last.then_inc(post_multiplied, 1)

            def chunk(hop, c, before):
                g = hop * CHUNKS + c
                for k in range(TILES):
                    j, i = k // (STREAMED + 1), k % (STREAMED + 1)
                    if isinstance(c, int) and i == 0:
                        pe.wait_ge(taken_over, hop * CHUNKS + j + 1)
                    if k == POST_AT and before:
                        post(*before)
                    y_high, y_low = operand_high[:, hop % 2, k, :], operand_low[:, hop % 2, k, :]
                    out = sums[:, c, :]
                    if i < STREAMED:
                        n = j * STREAMED + i
                        a_high, a_low = ring_high[:, n % RING, :], ring_low[:, n % RING, :]
                        pe.wait_ge(high_ready, g * BLOCKS + n + 1)
                    else:
                        a_high, a_low = resident_high[:, c, j, :], resident_low[:, c, j, :]
                        if hop == 0:
                            pe.wait_ge(resident_high_ready, c * GROUPS + j + 1)
                    nc.tensor.matmul(out, y_high, a_high, start=(k == 0), stop=False)
                    nc.tensor.matmul(out, y_low, a_high, start=False, stop=False)
                    if i < STREAMED:
                        pe.wait_ge(low_ready, g * BLOCKS + n + 1)
                    elif hop == 0:
                        pe.wait_ge(resident_low_ready, c * GROUPS + j + 1)
                    last = nc.tensor.matmul(out, y_high, a_low, start=False, stop=(k == TILES - 1))
                    if i < STREAMED:
                        last.then_inc(block_used, 1)
                last.then_inc(chunk_summed, 1)

            pe.wait_ge(params_in, 16)
            pe.wait_ge(x_t_in, 16)
            for g in range(CHUNKS):
                for t in range(g * TPC, (g + 1) * TPC):
                    last = nc.tensor.matmul(sums[:, g, t % TPC * D:(t % TPC + 1) * D], xt[:, t * P:(t + 1) * P],
                                            par[:, W1:W1 + D], start=True, stop=True)
                last.then_inc(first_multiplied, 1)
            pe.wait_ge(ident_ready, 1)
            for hop in range(HOPS):
                chunk(hop, 0, (hop - 1, CHUNKS - 1) if hop else None)
                with pe.Fori(1, CHUNKS) as c:
                    chunk(hop, c, (hop, c - 1))
            post(HOPS - 1, CHUNKS - 1)

        @block.scalar
        def _(act):
            def evacuate(hop, c):
                act.wait_ge(chunk_summed, hop * CHUNKS + c + 1)
                if hop <= 1:
                    b = (B1, B2)[hop]
                    nc.scalar.activation(chunk_t[:], sums[:, c, :], ACT.Relu, bias=par[:, b:b + 1]
                                         ).then_inc(chunk_evacuated, 1)
                else:
                    nc.scalar.activation(chunk_t[:], sums[:, c, :], ACT.Copy).then_inc(chunk_evacuated, 1)

            def deviations(n):
                act.wait_ge(norm_step, n * NORM_STEPS + 3)
                nc.scalar.activation(deviation[:], moments[:, :, 1], ACT.Sqrt).then_inc(deviation_ready, 1)

            def operand_tiles(hop, c):
                if hop == 1:
                    act.wait_ge(norm_step, (c + 1) * NORM_STEPS)
                    source = nodes[:, bass.ts(c, TPC), :]
                else:
                    act.wait_ge(post_multiplied, hop * CHUNKS + c + 1)
                    source = weighted[:] if hop == 0 else turned[:]
                nc.scalar.activation(operand_high[:, (hop + 1) % 2, bass.ts(c, TPC), :], source, ACT.Copy
                                     ).then_inc(operand_high_ready, 1)

            def chunk(hop, c, before):
                g = hop * CHUNKS + c
                for n in range(BLOCKS):
                    if before:
                        if n == EVACUATE_AT:
                            evacuate(*before)
                        if n == 6 and before[0] in (0, 2, 3):
                            operand_tiles(*before)
                        if n == 9 and before[0] in NORMED:
                            deviations(before[1] + (CHUNKS if before[0] == 4 else 0))
                        if n == 11 and before[0] == 1:
                            operand_tiles(*before)
                    j, i = n // STREAMED, n % STREAMED
                    if hop == 0 and i == 0:
                        act.wait_ge(adj_in[j], 32 * c + 32)
                    if before or n >= RING:
                        act.wait_ge(block_used, g * BLOCKS + n - RING + 1)
                    nc.scalar.activation(ring_high[:, n % RING, :], adj[:, c, n, :], ACT.Copy).then_inc(high_ready, 1)
                    if hop == 0 and i == STREAMED - 1:
                        nc.scalar.activation(resident_high[:, c, j, :], staged[:, j, :], ACT.Copy
                                             ).then_inc(resident_high_ready, 1)

            for g in range(CHUNKS):
                act.wait_ge(first_multiplied, g + 1)
                nc.scalar.activation(operand_high[:, 0, g * TPC:(g + 1) * TPC, :], sums[:, g, :], ACT.Copy
                                     ).then_inc(operand_high_ready, 1)
            for hop in range(HOPS):
                chunk(hop, 0, (hop - 1, CHUNKS - 1) if hop else None)
                with act.Fori(1, CHUNKS) as c:
                    chunk(hop, c, (hop, c - 1))
            evacuate(HOPS - 1, CHUNKS - 1)
            deviations(2 * CHUNKS - 1)

        @block.vector
        def _(dve):
            def residual(c):
                group = nodes[:, c * TPC:(c + 1) * TPC, :]
                dve.wait_ge(post_multiplied, CHUNKS + c + 1)
                nc.vector.tensor_tensor(group, turned[:], group, ALU.add).then_inc(residual_added, 1)

            def add_products(hop, c):
                group = nodes[:, bass.ts(c, TPC), :]
                dve.wait_ge(post_multiplied, hop * CHUNKS + c + 1)
                nc.vector.scalar_tensor_tensor(group, weighted[:], 1.0 / 3.0, group, ALU.mult, ALU.add
                                               ).then_inc(taken_over, 1)

            def norm_stats(hop, c):
                n = c if hop == 1 else c + CHUNKS
                if hop == 1:
                    dve.wait_ge(residual_added, c + 1)
                else:
                    dve.wait_ge(taken_over, (hop + 1) * CHUNKS + c + 1)
                for t in range(TPC):
                    last = nc.vector.bn_stats(stats[:, t, :], nodes[:, c * TPC + t, :])
                last.then_inc(norm_step, 1)

            def norm_moments(hop, c):
                n = c if hop == 1 else c + CHUNKS
                dve.wait_ge(norm_step, n * NORM_STEPS + 1)
                for t in range(TPC):
                    last = nc.vector.bn_aggr(moments[:, t, :], stats[:, t, :])
                last.then_inc(norm_step, 1)
                dve.wait_ge(norm_step, n * NORM_STEPS + 2)
                nc.vector.tensor_scalar(moments[:, :, 1], moments[:, :, 1], EPS, None, ALU.add).then_inc(norm_step, 1)

            def norm_apply(hop, c):
                n = c if hop == 1 else c + CHUNKS
                dve.wait_ge(deviation_ready, n + 1)
                nc.vector.reciprocal(rstd[:], deviation[:]).then_inc(norm_step, 1)
                dve.wait_ge(norm_step, n * NORM_STEPS + 4)
                for t in range(TPC):
                    tile = nodes[:, c * TPC + t, :]
                    last = nc.vector.tensor_scalar(tile, tile, moments[:, t, 0:1], rstd[:, t:t + 1],
                                                   ALU.subtract, ALU.mult)
                last.then_inc(norm_step, 1)

            def operand_tiles(hop, c):
                dve.wait_ge(operand_high_ready, (hop + 1) * CHUNKS + c + 1)
                high, low = (o[:, (hop + 1) % 2, bass.ts(c, TPC), :] for o in (operand_high, operand_low))
                source = {0: weighted[:], 1: nodes[:, bass.ts(c, TPC), :]}.get(hop, turned[:])
                split = nc.vector.tensor_tensor(low, source, high.bitcast(F32), ALU.subtract)
                if hop < 2:
                    split.then_inc(taken_over, 1)

            def post_step(n, hop, c):
                if hop == 1:
                    {6: residual, 7: lambda c: norm_stats(1, c), 8: lambda c: norm_moments(1, c),
                     9: lambda c: norm_apply(1, c), 11: lambda c: operand_tiles(1, c)}.get(n, lambda c: None)(c)
                elif hop == 4:
                    {6: add_products, 7: norm_stats, 8: norm_moments, 9: norm_apply}.get(n, lambda h, c: None)(4, c)
                elif n == 6:
                    operand_tiles(hop, c)
                elif n == 7 and hop >= 2:
                    add_products(hop, c)

            def chunk(hop, c, before):
                g = hop * CHUNKS + c
                for n in range(BLOCKS):
                    if before:
                        post_step(n, *before)
                    j, i = n // STREAMED, n % STREAMED
                    dve.wait_ge(high_ready, g * BLOCKS + n + 1)
                    nc.vector.tensor_tensor(ring_low[:, n % RING, :], adj[:, c, n, :],
                                            ring_high[:, n % RING, :].bitcast(F32), ALU.subtract).then_inc(low_ready, 1)
                    if hop == 0 and i == STREAMED - 1:
                        dve.wait_ge(resident_high_ready, c * GROUPS + j + 1)
                        nc.vector.tensor_tensor(resident_low[:, c, j, :], staged[:, j, :],
                                                resident_high[:, c, j, :].bitcast(F32), ALU.subtract
                                                ).then_inc(resident_low_ready, 1)

            for g in range(CHUNKS):
                dve.wait_ge(operand_high_ready, g + 1)
                high, low = (o[:, 0, g * TPC:(g + 1) * TPC, :] for o in (operand_high, operand_low))
                nc.vector.tensor_tensor(low, sums[:, g, :], high.bitcast(F32), ALU.subtract).then_inc(taken_over, 1)
            for hop in range(HOPS):
                if hop == 1:
                    dve.wait_ge(x_in, 16)
                chunk(hop, 0, (hop - 1, CHUNKS - 1) if hop else None)
                if hop in NORMED:
                    for c in range(1, CHUNKS):
                        chunk(hop, c, (hop, c - 1))
                else:
                    with dve.Fori(1, CHUNKS) as c:
                        chunk(hop, c, (hop, c - 1))
            for n in range(BLOCKS):
                post_step(n, HOPS - 1, CHUNKS - 1)


def kernel(x, adj, L0_gnn_W1, L0_gnn_b1, L0_gnn_W2, L0_gnn_b2, L1_gnn_W1, L1_gnn_W2, L1_gnn_W3):
    import numpy as np
    import concourse.bacc as bacc
    from concourse.bass_utils import run_bass_kernel_spmd

    x, adj = np.asarray(x), np.asarray(adj)
    arrays = {
        "a_t": adj.reshape(CHUNKS, CHUNK, TILES, P).transpose(0, 3, 2, 1),
        "x_t": x.T,
        "x_rows": x.reshape(TILES, P, D).transpose(1, 0, 2),
        "params": np.concatenate([np.asarray(L0_gnn_W1), np.asarray(L0_gnn_W2), np.asarray(L1_gnn_W1),
                                  np.asarray(L1_gnn_W2), np.asarray(L1_gnn_W3),
                                  np.asarray(L0_gnn_b1)[:, None], np.asarray(L0_gnn_b2)[:, None]], axis=1),
    }
    arrays = {name: np.ascontiguousarray(a) for name, a in arrays.items()}
    nc = bacc.Bacc("TRN2", target_bir_lowering=False, num_devices=1, dynamic_dma_scratch_size=1024)
    ins = [nc.dram_tensor(name, a.shape, F32, kind="ExternalInput").ap() for name, a in arrays.items()]
    out_rows = nc.dram_tensor("out_rows", (P, TILES, D), F32, kind="ExternalOutput").ap()
    graph_layers(nc, *ins, out_rows)
    r = run_bass_kernel_spmd(nc, [arrays], core_ids=[0])
    return np.asarray(r.results[0]["out_rows"]).transpose(1, 0, 2).reshape(N, D)
```

```python
from contextlib import ExitStack

import concourse.bass as bass
from concourse import mybir

P = 128
N = 2048
D = 128
TILES = N // P
CHUNK = 512
CHUNKS = N // CHUNK
TPC = CHUNK // P
GROUPS = 4
STREAMED = TILES // GROUPS - 1
BLOCKS = GROUPS * STREAMED
RING = 4
HOPS = 5
NORMED = (1, 4)
WEIGHTED = (0, 2, 3, 4)
TURNED = (1, 2, 3)
POST_AT = 2
ACT_STEPS = {
    0: {2: ["evacuate"], 6: ["operand"]},
    1: {4: ["evacuate"], 11: ["operand"]},
    2: {4: ["evacuate"], 6: ["operand"]},
    3: {4: ["evacuate"], 6: ["operand"]},
    4: {4: ["evacuate"]},
}
DVE_STEPS = {
    0: {6: ["operand"]},
    1: {5: ["residual"], 6: ["stats"], 7: ["moments"], 9: ["apply"], 11: ["operand"]},
    2: {6: ["operand"], 7: ["products"]},
    3: {6: ["operand"], 7: ["products"]},
    4: {6: ["products", "stats"], 7: ["moments"], 9: ["apply"]},
}
NORM_STEPS = 4
HALVES = 2
EPS = 1e-5
assert BLOCKS % RING == 0 and TPC == GROUPS == CHUNKS

F32 = mybir.dt.float32
F32R = mybir.dt.float32r
ALU = mybir.AluOpType
ACT = mybir.ActivationFunctionType

W1, W2, B1, B2 = 0, D, 2 * D, 2 * D + 1
V1 = B2 + 1
V2, V3, PARAMS = V1 + D, V1 + 2 * D, V1 + 3 * D


def graph_layers(nc: bass.Bass, a_t, x_t, x_rows, params, out_rows):
    with ExitStack() as ctx:
        def sb(name, shape, dt=F32):
            return ctx.enter_context(nc.sbuf_tensor(name, shape, dt))

        def psum(name, shape, dt=F32):
            return ctx.enter_context(nc.psum_tensor(name, shape, dt))

        def sem(name):
            return ctx.enter_context(nc.semaphore(name))

        adj = sb("adj", [P, CHUNKS, BLOCKS, CHUNK])
        resident_high = sb("resident_high", [P, CHUNKS, GROUPS, CHUNK], F32R)
        resident_low = sb("resident_low", [P, CHUNKS, GROUPS, CHUNK], F32R)
        ring_high = sb("ring_high", [P, RING, CHUNK], F32R)
        ring_low = sb("ring_low", [P, RING, CHUNK], F32R)
        operand_high = sb("operand_high", [P, 2, TILES, D], F32R)
        operand_low = sb("operand_low", [P, 2, TILES, D], F32R)
        nodes = sb("nodes", [P, TILES, D])
        par = sb("par", [P, PARAMS])
        ident = sb("ident", [P, P])
        chunk_t = sb("chunk_t", [P, CHUNK])
        stats = sb("stats", [P, TPC, 6])
        moments = sb("moments", [P, TPC, 2])
        variance = sb("variance", [P, TPC])
        exponent = sb("exponent", [P, TPC])
        rstd = sb("rstd", [P, TPC])
        xt = nodes[:].rearrange("p t d -> p (t d)")
        staged = nodes[:].rearrange("p (j t) d -> p j (t d)", j=GROUPS)

        sums = psum("sums", [P, CHUNKS, CHUNK])
        turned = psum("turned", [P, TPC, D])
        weighted = psum("weighted", [P, TPC, D])

        first_banks = [sums[:, 1, :], sums[:, 2, :], sums[:, 3, :], turned[:].rearrange("p t d -> p (t d)")]

        adj_in = [sem(f"adj_in{n}") for n in range(BLOCKS)]
        staged_in = [sem(f"staged_in{j}") for j in range(GROUPS)]
        x_t_in = [sem(f"x_t_in{g}") for g in range(CHUNKS)]
        w1_in = sem("w1_in")
        x_in = sem("x_in")
        layer_0_in = sem("layer_0_in")
        layer_1_in = sem("layer_1_in")
        ident_zero = sem("ident_zero")
        ident_ready = sem("ident_ready")
        high_ready = sem("high_ready")
        low_ready = sem("low_ready")
        high_used = sem("high_used")
        low_used = sem("low_used")
        resident_high_ready = sem("resident_high_ready")
        resident_low_ready = sem("resident_low_ready")
        first_multiplied = sem("first_multiplied")
        chunk_summed = sem("chunk_summed")
        chunk_evacuated = sem("chunk_evacuated")
        post_multiplied = sem("post_multiplied")
        operand_high_ready = sem("operand_high_ready")
        taken_over = sem("taken_over")
        residual_added = sem("residual_added")
        norm_step = sem("norm_step")
        exponent_ready = sem("exponent_ready")
        rstd_ready = sem("rstd_ready")
        out_stored = sem("out_stored")

        block = ctx.enter_context(nc.Block())

        half_tiles = TPC // HALVES
        last_hop_groups = [slice(c * TPC, (c + 1) * TPC) for c in range(CHUNKS - 1)]
        last_hop_groups += [slice(t, t + half_tiles) for t in range(TILES - TPC, TILES, half_tiles)]
        last_banks = [weighted, turned]

        whole_groups = len(NORMED) * CHUNKS - 1

        def measured(n):
            if isinstance(n, int) and n > whole_groups:
                return measured(n - 1) + NORM_STEPS - 1
            return n * NORM_STEPS + 3

        def applied(n):
            return n * NORM_STEPS + NORM_STEPS if n < whole_groups else measured(whole_groups + HALVES - 1) + n - whole_groups + 1

        @block.sync
        def _(sp):
            def load_streamed(c, n):
                k = n // STREAMED * (STREAMED + 1) + n % STREAMED
                sp.dma_start(adj[:, c, n, :], a_t[c, :, k, :]).then_inc(adj_in[n], 16)

            def load_staged(c, j):
                sp.dma_start(staged[:, j, :], a_t[c, :, j * (STREAMED + 1) + STREAMED, :]).then_inc(staged_in[j], 16)

            sp.dma_start(par[:, W1:W1 + D], params[:, W1:W1 + D]).then_inc(w1_in, 16)
            for g in range(CHUNKS):
                part = slice(g * CHUNK, (g + 1) * CHUNK)
                sp.dma_start(xt[:, part], x_t[:, part]).then_inc(x_t_in[g], 16)
            for n in range(BLOCKS):
                load_streamed(0, n)
                if n % STREAMED == STREAMED - 1:
                    sp.wait_ge(first_multiplied, n // STREAMED + 1)
                    load_staged(0, n // STREAMED)
            sp.dma_start(par[:, W2:V1], params[:, W2:V1]).then_inc(layer_0_in, 16)
            for c in range(1, CHUNKS):
                for n in range(BLOCKS):
                    sp.wait_ge(adj_in[n], 16 * c)
                    load_streamed(c, n)
                    if n % STREAMED == STREAMED - 1:
                        sp.wait_ge(resident_low_ready, (c - 1) * GROUPS + n // STREAMED + 1)
                        load_staged(c, n // STREAMED)
            sp.dma_start(par[:, V1:], params[:, V1:]).then_inc(layer_1_in, 16)
            sp.wait_ge(resident_low_ready, CHUNKS * GROUPS)
            sp.dma_start(nodes[:], x_rows).then_inc(x_in, 16)
            for n, tiles in enumerate(last_hop_groups):
                sp.wait_ge(norm_step, applied(CHUNKS + n))
                sp.dma_start(out_rows[:, tiles, :], nodes[:, tiles, :]).then_inc(out_stored, 16)
            sp.wait_ge(out_stored, 16 * len(last_hop_groups))

        @block.gpsimd
        def _(pool):
            nc.gpsimd.memset(ident[:], 0.0).then_inc(ident_zero, 1)
            pool.wait_ge(ident_zero, 1)
            nc.gpsimd.affine_select(out=ident[:], in_=ident[:], compare_op=ALU.not_equal, fill=1.0, base=0,
                                    pattern=[[-1, P]], channel_multiplier=1).then_inc(ident_ready, 1)
            nc.gpsimd.memset(exponent[:], -0.5).then_inc(exponent_ready, 1)
            pool.wait_ge(exponent_ready, 1)
            with pool.Fori(0, whole_groups) as n:
                pool.wait_ge(norm_step, measured(n))
                nc.gpsimd.tensor_tensor(rstd[:], variance[:], exponent[:], ALU.pow).then_inc(rstd_ready, 1)
            for half in range(HALVES):
                part = slice(half * half_tiles, (half + 1) * half_tiles)
                pool.wait_ge(norm_step, measured(whole_groups + half))
                nc.gpsimd.tensor_tensor(rstd[:, part], variance[:, part], exponent[:, part], ALU.pow
                                        ).then_inc(rstd_ready, 1)

        @block.tensor
        def _(pe):
            def post(hop, c):
                g = hop * CHUNKS + c
                pe.wait_ge(chunk_evacuated, g + 1)
                if hop == 2:
                    pe.wait_ge(layer_1_in, 16)
                pe.wait_ge(taken_over, CHUNKS + g)
                for t in range(TPC):
                    tile = chunk_t[:, t * P:(t + 1) * P]
                    if hop in TURNED:
                        last = nc.tensor.transpose(turned[:, t, :], tile, ident[:])
                    if hop in WEIGHTED:
                        w = {0: W2, 2: V1, 3: V2, 4: V3}[hop]
                        last = nc.tensor.matmul(weighted[:, t, :], tile, par[:, w:w + D], start=True, stop=True)
                last.then_inc(post_multiplied, 1)

            def first_product(g):
                pe.wait_ge(x_t_in[g], 16)
                for t in range(TPC):
                    k = g * TPC + t
                    last = nc.tensor.matmul(first_banks[g][:, t * D:(t + 1) * D], xt[:, k * P:(k + 1) * P],
                                            par[:, W1:W1 + D], start=True, stop=True)
                last.then_inc(first_multiplied, 1)

            def low_product(hop, c, k):
                j, i = k // (STREAMED + 1), k % (STREAMED + 1)
                if i < STREAMED:
                    n = j * STREAMED + i
                    a_low = ring_low[:, n % RING, :]
                    pe.wait_ge(low_ready, (hop * CHUNKS + c) * BLOCKS + n + 1)
                else:
                    a_low = resident_low[:, c, j, :]
                    if hop == 0:
                        pe.wait_ge(resident_low_ready, c * GROUPS + j + 1)
                used = nc.tensor.matmul(sums[:, c, :], operand_high[:, hop % 2, k, :], a_low,
                                        start=False, stop=(k == TILES - 1))
                if i < STREAMED:
                    used.then_inc(low_used, 1)
                return used

            def chunk(hop, c, before):
                g = hop * CHUNKS + c
                for k in range(TILES):
                    j, i = k // (STREAMED + 1), k % (STREAMED + 1)
                    if isinstance(c, int) and i == 0:
                        pe.wait_ge(taken_over, hop * CHUNKS + j + 1)
                    if k == POST_AT and before:
                        post(*before)
                    y_high, y_low = operand_high[:, hop % 2, k, :], operand_low[:, hop % 2, k, :]
                    if i < STREAMED:
                        n = j * STREAMED + i
                        a_high = ring_high[:, n % RING, :]
                        pe.wait_ge(high_ready, g * BLOCKS + n + 1)
                    else:
                        a_high = resident_high[:, c, j, :]
                        if hop == 0:
                            pe.wait_ge(resident_high_ready, c * GROUPS + j + 1)
                    nc.tensor.matmul(sums[:, c, :], y_high, a_high, start=(k == 0), stop=False)
                    used = nc.tensor.matmul(sums[:, c, :], y_low, a_high, start=False, stop=False)
                    if i < STREAMED:
                        used.then_inc(high_used, 1)
                    if k >= 1:
                        low_product(hop, c, k - 1)
                last = low_product(hop, c, TILES - 1)
                last.then_inc(chunk_summed, 1)

            pe.wait_ge(w1_in, 16)
            for g in range(CHUNKS):
                first_product(g)
            pe.wait_ge(ident_ready, 1)
            for hop in range(HOPS):
                chunk(hop, 0, (hop - 1, CHUNKS - 1) if hop else None)
                with pe.Fori(1, CHUNKS) as c:
                    chunk(hop, c, (hop, c - 1))
            pe.wait_ge(taken_over, HOPS * CHUNKS + CHUNKS - 1)
            for half in range(HALVES):
                pe.wait_ge(chunk_evacuated, HOPS * CHUNKS + half)
                for t in range(half_tiles):
                    k = half * half_tiles + t
                    last = nc.tensor.matmul(last_banks[half][:, t, :], chunk_t[:, k * P:(k + 1) * P],
                                            par[:, V3:V3 + D], start=True, stop=True)
                last.then_inc(post_multiplied, 1)

        @block.scalar
        def _(act):
            def evacuate(hop, c):
                if hop == 0:
                    act.wait_ge(layer_0_in, 16)
                act.wait_ge(chunk_summed, hop * CHUNKS + c + 1)
                if hop <= 1:
                    b = (B1, B2)[hop]
                    nc.scalar.activation(chunk_t[:], sums[:, c, :], ACT.Relu, bias=par[:, b:b + 1]
                                         ).then_inc(chunk_evacuated, 1)
                else:
                    nc.scalar.activation(chunk_t[:], sums[:, c, :], ACT.Copy).then_inc(chunk_evacuated, 1)

            def post_step(n, hop, c):
                for step in ACT_STEPS[hop].get(n, ()):
                    if step == "evacuate":
                        evacuate(hop, c)
                    else:
                        operand_tiles(hop, c)

            def operand_tiles(hop, c):
                if hop == 1:
                    act.wait_ge(norm_step, (c + 1) * NORM_STEPS)
                    source = nodes[:, bass.ts(c, TPC), :]
                else:
                    act.wait_ge(post_multiplied, hop * CHUNKS + c + 1)
                    source = weighted[:] if hop == 0 else turned[:]
                nc.scalar.activation(operand_high[:, (hop + 1) % 2, bass.ts(c, TPC), :], source, ACT.Copy
                                     ).then_inc(operand_high_ready, 1)

            def first_tiles(g):
                act.wait_ge(first_multiplied, g + 1)
                nc.scalar.activation(operand_high[:, 0, g * TPC:(g + 1) * TPC, :], first_banks[g], ACT.Copy
                                     ).then_inc(operand_high_ready, 1)

            def chunk(hop, c, before):
                g = hop * CHUNKS + c
                for n in range(BLOCKS):
                    if before:
                        post_step(n, *before)
                    j, i = n // STREAMED, n % STREAMED
                    if hop == 0:
                        if i == 0 and not before:
                            first_tiles(j)
                        act.wait_ge(adj_in[n], 16 * c + 16)
                    if before or n >= RING:
                        act.wait_ge(high_used, g * BLOCKS + n - RING + 1)
                        act.wait_ge(low_ready, g * BLOCKS + n - RING + 1)
                    nc.scalar.activation(ring_high[:, n % RING, :], adj[:, c, n, :], ACT.Copy).then_inc(high_ready, 1)
                    if hop == 0 and i == STREAMED - 1:
                        act.wait_ge(staged_in[j], 16 * c + 16)
                        nc.scalar.activation(resident_high[:, c, j, :], staged[:, j, :], ACT.Copy
                                             ).then_inc(resident_high_ready, 1)

            for hop in range(HOPS):
                chunk(hop, 0, (hop - 1, CHUNKS - 1) if hop else None)
                with act.Fori(1, CHUNKS) as c:
                    chunk(hop, c, (hop, c - 1))
            act.wait_ge(chunk_summed, HOPS * CHUNKS)
            for half in range(HALVES):
                part = slice(half * half_tiles * P, (half + 1) * half_tiles * P)
                nc.scalar.activation(chunk_t[:, part], sums[:, CHUNKS - 1, part], ACT.Copy).then_inc(chunk_evacuated, 1)

        @block.vector
        def _(dve):
            def residual(c):
                group = nodes[:, c * TPC:(c + 1) * TPC, :]
                dve.wait_ge(x_in, 16)
                dve.wait_ge(post_multiplied, CHUNKS + c + 1)
                nc.vector.tensor_tensor(group, turned[:], group, ALU.add).then_inc(residual_added, 1)

            def add_products(hop, c):
                group = nodes[:, bass.ts(c, TPC), :]
                dve.wait_ge(post_multiplied, hop * CHUNKS + c + 1)
                nc.vector.scalar_tensor_tensor(group, weighted[:], 1.0 / 3.0, group, ALU.mult, ALU.add
                                               ).then_inc(taken_over, 1)

            def norm_stats(tiles):
                for t, tile in enumerate(tiles):
                    last = nc.vector.bn_stats(stats[:, t, :], nodes[:, tile, :])
                last.then_inc(norm_step, 1)

            def norm_moments(n, tiles, at=0):
                dve.wait_ge(norm_step, measured(n) - 2)
                for t in range(len(tiles)):
                    last = nc.vector.bn_aggr(moments[:, at + t, :], stats[:, t, :])
                last.then_inc(norm_step, 1)
                dve.wait_ge(norm_step, measured(n) - 1)
                nc.vector.tensor_scalar(variance[:, at:at + len(tiles)], moments[:, at:at + len(tiles), 1], EPS, None,
                                        ALU.add).then_inc(norm_step, 1)

            def norm_apply(n, tiles, at=0):
                dve.wait_ge(rstd_ready, n + 1)
                for t, tile in enumerate(tiles):
                    t += at
                    last = nc.vector.tensor_scalar(nodes[:, tile, :], nodes[:, tile, :], moments[:, t, 0:1],
                                                   rstd[:, t:t + 1], ALU.subtract, ALU.mult)
                last.then_inc(norm_step, 1)

            def operand_tiles(hop, c):
                dve.wait_ge(operand_high_ready, (hop + 1) * CHUNKS + c + 1)
                high, low = (o[:, (hop + 1) % 2, bass.ts(c, TPC), :] for o in (operand_high, operand_low))
                source = {0: weighted[:], 1: nodes[:, bass.ts(c, TPC), :]}.get(hop, turned[:])
                split = nc.vector.tensor_tensor(low, source, high.bitcast(F32), ALU.subtract)
                if hop < 2:
                    split.then_inc(taken_over, 1)

            def post_step(n, hop, c):
                for step in DVE_STEPS[hop].get(n, ()):
                    if step == "residual":
                        residual(c)
                    elif step == "operand":
                        operand_tiles(hop, c)
                    elif step == "products":
                        add_products(hop, c)
                    elif step == "stats":
                        if hop == 1:
                            dve.wait_ge(residual_added, c + 1)
                        else:
                            dve.wait_ge(taken_over, (hop + 1) * CHUNKS + c + 1)
                        norm_stats(range(c * TPC, (c + 1) * TPC))
                    else:
                        n = c if hop == 1 else CHUNKS + c
                        {"moments": norm_moments, "apply": norm_apply}[step](n, range(c * TPC, (c + 1) * TPC))

            def first_tiles(g):
                dve.wait_ge(operand_high_ready, g + 1)
                high, low = (o[:, 0, g * TPC:(g + 1) * TPC, :] for o in (operand_high, operand_low))
                nc.vector.tensor_tensor(low, first_banks[g], high.bitcast(F32), ALU.subtract).then_inc(taken_over, 1)

            def chunk(hop, c, before):
                g = hop * CHUNKS + c
                for n in range(BLOCKS):
                    if before:
                        post_step(n, *before)
                    j, i = n // STREAMED, n % STREAMED
                    if hop == 0 and i == 0 and not before:
                        first_tiles(j)
                    if before or n >= RING:
                        dve.wait_ge(low_used, g * BLOCKS + n - RING + 1)
                    dve.wait_ge(high_ready, g * BLOCKS + n + 1)
                    nc.vector.tensor_tensor(ring_low[:, n % RING, :], adj[:, c, n, :],
                                            ring_high[:, n % RING, :].bitcast(F32), ALU.subtract).then_inc(low_ready, 1)
                    if hop == 0 and i == STREAMED - 1:
                        dve.wait_ge(resident_high_ready, c * GROUPS + j + 1)
                        nc.vector.tensor_tensor(resident_low[:, c, j, :], staged[:, j, :],
                                                resident_high[:, c, j, :].bitcast(F32), ALU.subtract
                                                ).then_inc(resident_low_ready, 1)

            for hop in range(HOPS):
                chunk(hop, 0, (hop - 1, CHUNKS - 1) if hop else None)
                if hop in NORMED:
                    for c in range(1, CHUNKS):
                        chunk(hop, c, (hop, c - 1))
                else:
                    with dve.Fori(1, CHUNKS) as c:
                        chunk(hop, c, (hop, c - 1))
            groups = [range(t.start, t.stop) for t in last_hop_groups[-HALVES:]]
            for half, tiles in enumerate(groups):
                added = nodes[:, tiles.start:tiles.stop, :]
                dve.wait_ge(post_multiplied, HOPS * CHUNKS + half)
                nc.vector.scalar_tensor_tensor(added, last_banks[half][:, 0:half_tiles, :], 1.0 / 3.0, added,
                                               ALU.mult, ALU.add).then_inc(taken_over, 1)
                dve.wait_ge(taken_over, (HOPS + 1) * CHUNKS + half)
                norm_stats(tiles)
                norm_moments(whole_groups + half, tiles, half * half_tiles)
            for half, tiles in enumerate(groups):
                norm_apply(whole_groups + half, tiles, half * half_tiles)


def kernel(x, adj, L0_gnn_W1, L0_gnn_b1, L0_gnn_W2, L0_gnn_b2, L1_gnn_W1, L1_gnn_W2, L1_gnn_W3):
    import numpy as np
    import concourse.bacc as bacc
    from concourse.bass_utils import run_bass_kernel_spmd

    x, adj = np.asarray(x), np.asarray(adj)
    arrays = {
        "a_t": adj.reshape(CHUNKS, CHUNK, TILES, P).transpose(0, 3, 2, 1),
        "x_t": x.T,
        "x_rows": x.reshape(TILES, P, D).transpose(1, 0, 2),
        "params": np.concatenate([np.asarray(L0_gnn_W1), np.asarray(L0_gnn_W2),
                                  np.asarray(L0_gnn_b1)[:, None], np.asarray(L0_gnn_b2)[:, None],
                                  np.asarray(L1_gnn_W1), np.asarray(L1_gnn_W2), np.asarray(L1_gnn_W3)], axis=1),
    }
    arrays = {name: np.ascontiguousarray(a) for name, a in arrays.items()}
    nc = bacc.Bacc("TRN2", target_bir_lowering=False, num_devices=1, dynamic_dma_scratch_size=1024)
    ins = [nc.dram_tensor(name, a.shape, F32, kind="ExternalInput").ap() for name, a in arrays.items()]
    out_rows = nc.dram_tensor("out_rows", (P, TILES, D), F32, kind="ExternalOutput").ap()
    graph_layers(nc, *ins, out_rows)
    r = run_bass_kernel_spmd(nc, [arrays], core_ids=[0])
    return np.asarray(r.results[0]["out_rows"]).transpose(1, 0, 2).reshape(N, D)
```
